# Optimizing a Trainium2 kernel written in Bass

```python
import numpy as np
import jax
import jax.numpy as jnp

def _softmax(x, axis=-1):
    return jax.nn.softmax(x, axis=axis)

def _gelu(x):
    return jax.nn.gelu(x, approximate=True)

def _silu(x):
    return jax.nn.silu(x)

def _sigmoid(x):
    return jax.nn.sigmoid(x)

def _layernorm(x, axis=-1, eps=1e-05):
    m = jnp.mean(x, axis=axis, keepdims=True)
    v = jnp.var(x, axis=axis, keepdims=True)
    return (x - m) / jnp.sqrt(v + eps)

def _scatter_add(tgt, idx, src, axis=0):
    return tgt.at[idx].add(src)

def _segment_sum(src, seg, n):
    return jax.ops.segment_sum(src, seg, n)
kernel_name = 'mk_sandwich_d1_jaxref_r4_945dd7'

def setup_inputs(seed: int=0):
    np.random.seed(seed)
    _w = jnp.asarray

    def _L0_attn_setup():
        import jax, jax.numpy as jnp
        import numpy as np
        EMBED_DIM = 256
        NUM_HEADS = 16
        BLOCK_SIZE = 128
        GLOBAL_EVERY = 24

        def make_block_sparse_mask(seq_len):
            bi = jnp.arange(seq_len) // BLOCK_SIZE
            is_global = bi % GLOBAL_EVERY == 0
            allowed = (bi[:, None] == bi[None, :]) | is_global[:, None] | is_global[None, :]
            return jnp.where(allowed, 0.0, -jnp.inf).astype(jnp.float32)
        key = jax.random.key(seed)
        k_x, k_w, k_wo = jax.random.split(key, 3)
        B, L, D = (1, 1024, EMBED_DIM)
        x = jax.random.normal(k_x, (B, L, D), dtype=jnp.float32)
        w_qkv = jax.random.normal(k_w, (3 * D, D), dtype=jnp.float32) * 0.02
        b_qkv = jnp.zeros((3 * D,), dtype=jnp.float32)
        w_out = jax.random.normal(k_wo, (D, D), dtype=jnp.float32) * 0.02
        b_out = jnp.zeros((D,), dtype=jnp.float32)
        return {'x': x, 'w_qkv': w_qkv, 'b_qkv': b_qkv, 'w_out': w_out, 'b_out': b_out}
    _L0_attn_in = _L0_attn_setup()

    def _L0_ffn_setup():
        import jax, jax.numpy as jnp
        import numpy as np
        HIDDEN = 256
        INTER = 1024
        key = jax.random.key(seed)
        k1, k2, k3, k4, k5 = jax.random.split(key, 5)
        hidden_states = jax.random.normal(k1, (4, 512, HIDDEN), dtype=jnp.float32)
        W1 = jax.random.normal(k2, (HIDDEN, INTER), dtype=jnp.float32) * (1.0 / np.sqrt(HIDDEN))
        b1 = jax.random.normal(k3, (INTER,), dtype=jnp.float32) * 0.02
        W2 = jax.random.normal(k4, (INTER, HIDDEN), dtype=jnp.float32) * (1.0 / np.sqrt(INTER))
        b2 = jax.random.normal(k5, (HIDDEN,), dtype=jnp.float32) * 0.02
        return {'hidden_states': hidden_states, 'W1': W1, 'b1': b1, 'W2': W2, 'b2': b2}
    _L0_ffn_in = _L0_ffn_setup()
    _d = {'L0_attn_x': _L0_attn_in['x'], 'L0_attn_w_qkv': _L0_attn_in['w_qkv'], 'L0_attn_b_qkv': _L0_attn_in['b_qkv'], 'L0_attn_w_out': _L0_attn_in['w_out'], 'L0_attn_b_out': _L0_attn_in['b_out'], 'L0_ffn_W1': _L0_ffn_in['W1'], 'L0_ffn_b1': _L0_ffn_in['b1'], 'L0_ffn_W2': _L0_ffn_in['W2'], 'L0_ffn_b2': _L0_ffn_in['b2']}
    _x0 = _d['L0_attn_x']
    _d['L0_attn_x'] = jax.random.normal(jax.random.fold_in(jax.random.key(seed), 1), (32, 512, 256), dtype=_x0.dtype)
    del _x0
    return _d

def reference(L0_attn_x, L0_attn_w_qkv, L0_attn_b_qkv, L0_attn_w_out, L0_attn_b_out, L0_ffn_W1, L0_ffn_b1, L0_ffn_W2, L0_ffn_b2):

    def _L0_attn_ref(x, w_qkv, b_qkv, w_out, b_out):
        import jax, jax.numpy as jnp
        import numpy as np
        EMBED_DIM = 256
        NUM_HEADS = 16
        BLOCK_SIZE = 128
        GLOBAL_EVERY = 24

        def make_block_sparse_mask(seq_len):
            bi = jnp.arange(seq_len) // BLOCK_SIZE
            is_global = bi % GLOBAL_EVERY == 0
            allowed = (bi[:, None] == bi[None, :]) | is_global[:, None] | is_global[None, :]
            return jnp.where(allowed, 0.0, -jnp.inf).astype(jnp.float32)
        B, L, D = x.shape
        H = NUM_HEADS
        hd = D // H
        mask = make_block_sparse_mask(L)
        qkv = x @ w_qkv.T + b_qkv
        q, k, v = jnp.split(qkv, 3, axis=-1)
        q = q.reshape(B, L, H, hd).transpose(0, 2, 1, 3)
        k = k.reshape(B, L, H, hd).transpose(0, 2, 1, 3)
        v = v.reshape(B, L, H, hd).transpose(0, 2, 1, 3)
        scale = 1.0 / jnp.sqrt(jnp.asarray(hd, dtype=x.dtype))
        scores = jnp.einsum('bhqd,bhkd->bhqk', q * scale, k) + mask
        attn = jax.nn.softmax(scores, axis=-1)
        out = jnp.einsum('bhqk,bhkd->bhqd', attn, v)
        out = out.transpose(0, 2, 1, 3).reshape(B, L, D)
        return out @ w_out.T + b_out

    def _L0_ffn_ref(hidden_states, W1, b1, W2, b2):
        import jax, jax.numpy as jnp
        import numpy as np
        HIDDEN = 256
        INTER = 1024
        h = jax.nn.relu(jnp.einsum('bsh,hi->bsi', hidden_states, W1) + b1)
        return jnp.einsum('bsi,ih->bsh', h, W2) + b2
    x = L0_attn_x
    x = x + _layernorm(_L0_attn_ref(_layernorm(x, axis=-1), L0_attn_w_qkv, L0_attn_b_qkv, L0_attn_w_out, L0_attn_b_out), axis=-1)
    x = x + _layernorm(_L0_ffn_ref(_layernorm(x, axis=-1), L0_ffn_W1, L0_ffn_b1, L0_ffn_W2, L0_ffn_b2), axis=-1)
    return x

_drawn_inputs = setup_inputs


def setup_inputs(seed=0):
    import zlib

    import numpy as np

    out = dict(_drawn_inputs(seed))
    spreads = {'L0_attn_b_qkv': (0.0, 0.1), 'L0_attn_b_out': (0.0, 0.1)}
    factors = {'L0_ffn_b1': 5.002, 'L0_ffn_b2': 3.379}
    for name, (base, spread) in spreads.items():
        noise = np.random.default_rng([zlib.crc32(name.encode()), seed]).standard_normal(out[name].shape)
        drawn = base * np.exp(spread * noise) if base else spread * noise
        out[name] = jnp.asarray(drawn.astype(out[name].dtype))
    for name, factor in factors.items():
        out[name] = (out[name] * factor).astype(out[name].dtype)
    return out
```

```python
import concourse.bass as bass
from concourse import mybir
from contextlib import ExitStack

F32 = mybir.dt.float32
F32R = mybir.dt.float32r
ALU = mybir.AluOpType
ACT = mybir.ActivationFunctionType
AX = mybir.AxisListType

SCHEDULE = {
    (0, 1): [("x2t", 0, -2), ("x2t", 1, -2)],
    (0, 2): [("lnf_stats", 1, -3)],
    (0, 3): [("f1", 0, -2), ("lnf_mean", 1, -3)],
    (0, 4): [("f1", 1, -2)],
    (1, 0): [("ot", 2, -1), ("lnf_apply", 1, -3)],
    (1, 1): [("qk", 2, 0)],
    (1, 2): [("qk", 3, 0), ("ln1_stats", 0, 1)],
    (1, 3): [("f1", 2, -2), ("ln1_mean", 0, 1)],
    (1, 4): [("f1", 3, -2), ("x1_keep", 0, -2), ("store", 1, -3)],
    (2, 0): [("load_xr", 0, -1)],
    (2, 2): [("f2", 0, -2)],
    (2, 3): [("ln1_apply", 0, 1)],
    (3, 0): [("ot", 3, -1)],
    (3, 1): [("v", 0, 0)],
    (3, 2): [("v", 1, 0)],
    (3, 3): [("f2", 1, -2)],
    (4, 1): [("x1t", 0, 1), ("x1t", 1, 1)],
    (4, 2): [("o2t", 0, -1), ("o2t", 1, -1), ("lnf_stats", 0, -2)],
    (4, 3): [("f1", 4, -2), ("lnf_mean", 0, -2), ("load_xa", 0, 2)],
    (4, 4): [("f1", 5, -2)],
    (5, 0): [("ot", 0, 0), ("lnf_apply", 0, -2)],
    (5, 1): [("qk", 0, 1)],
    (5, 2): [("qk", 1, 1)],
    (5, 3): [("op", 0, -1)],
    (5, 4): [("op", 1, -1), ("store", 0, -2)],
    (6, 0): [("lny_stats", 0, -1)],
    (6, 1): [("lny_mean", 0, -1)],
    (6, 2): [("f1", 6, -2), ("lny_apply", 0, -1)],
    (6, 4): [("f1", 7, -2)],
    (7, 0): [("ot", 1, 0), ("ln2_stats", 0, -1)],
    (7, 1): [("f2", 2, -2), ("ln2_mean", 0, -1)],
    (7, 2): [("ln2_apply", 0, -1)],
    (7, 3): [("f2", 3, -2)],
}
SLOTS, TURNS = 8, 5
LINEAR = {"x1t": 2, "x2t": 2, "o2t": 2, "qk": 4, "v": 2, "ot": 4, "op": 2, "f1": 8, "f2": 4}
UNITS = [job for s in range(SLOTS) for t in range(TURNS)
         for job in SCHEDULE.get((s, t), []) if job[0] in LINEAR]
AHEAD = 2
BEHIND = 3


def sandwich(nc, x, w_qkv_t, b_qk, b_v, w_out_t, b_out, w1, b1, w2, b2, out):
    NB, L, D = x.shape
    P = 128
    KB = L // P
    H, HD = 16, 16
    PAIRS = H // 2
    F = w1.shape[1]
    KD, KF = D // P, F // P
    HALF = L // 2
    VW = 32
    STACK = 4 * HD
    MAXROW = 96
    K_ALL = MAXROW + 2
    BUFS = 4
    CH = 5
    PC, QC = CH * PAIRS, KB * KB
    EPS = 1e-5
    SCALE = float(HD) ** -0.5
    PARTS = ((0, 0), (0, 1), (1, 0))
    O_QKV, O_W1 = 0, KD * 3 * D
    O_WO = O_W1 + KD * F
    O_W2 = O_WO + KD * D
    WCOLS = O_W2 + KF * D
    assert len(UNITS) % 2 == 0 and PC % 2 == 0

    x_t = x.rearrange("b (k p) d -> b p k d", p=P)
    out_t = out.rearrange("b (k p) d -> b p k d", p=P)

    with ExitStack() as ctx:
        def sb(name, shape, dt=F32):
            return ctx.enter_context(nc.sbuf_tensor(name, shape, dt))

        def ps(name, shape):
            return ctx.enter_context(nc.psum_tensor(name, shape, F32))

        def sem(name):
            return ctx.enter_context(nc.semaphore(name))

        w_hi, w_lo = sb("w_hi", [P, WCOLS], F32R), sb("w_lo", [P, WCOLS], F32R)
        w_parts = (w_hi, w_lo)
        ident = sb("ident", [P, P])
        bqk_s, b1_s = sb("bqk_s", [P, 4]), sb("b1_s", [P, KF])
        bv_s, bo_s, b2_s = sb("bv_s", [P, D]), sb("bo_s", [P, D]), sb("b2_s", [P, D])
        minus_half, eps = sb("minus_half", [P, KB]), sb("eps", [P, KB])
        xa = sb("xa", [P, KB, D])
        x1_t = [sb(f"x1_{n}", [P, KD, L], F32R) for n in ("hi", "lo")]
        qk = sb("qk", [P, 2, 4, L], F32R)
        stack = sb("stack", [P, BUFS, 2, 2, L], F32R)
        q_stack, k_stack = stack[:, :, 0, :, :], stack[:, :, 1, :, :]
        neg_max = sb("neg_max", [P, 2, KB, 2])
        max_row = sb("max_row", [2, 2, L])
        values = sb("values", [P, KB, H, VW])
        probs = sb("probs", [P, 2 * CH, L])
        o_t = sb("o_t", [P, L])
        den = sb("den", [P, KB, 4])
        o_n = sb("o_n", [P, KB, D])
        o2_t = [sb(f"o2_{n}", [P, KD, L], F32R) for n in ("hi", "lo")]
        ya = sb("ya", [P, KB, D])
        xr = sb("xr", [P, KB, D])
        xh = sb("xh", [P, KB, D])
        x2_t = [sb(f"x2_{n}", [P, KD, L], F32R) for n in ("hi", "lo")]
        x1_old = sb("x1_old", [P, KB, D])
        h_f = sb("h_f", [P, 2, 2, HALF])
        h_parts = [sb(f"h_{n}", [P, KF, HALF], F32R) for n in ("hi", "lo")]
        yf = sb("yf", [P, KB, D])
        KINDS = ("ln1", "lny", "ln2", "lnf")
        bn = {n: sb(f"bn_{n}", [P, KB, 6]) for n in KINDS}
        mv = {n: sb(f"mv_{n}", [P, KB, 2]) for n in KINDS}
        ve = {n: sb(f"ve_{n}", [P, KB]) for n in KINDS}
        rstd = {n: sb(f"rstd_{n}", [P, KB]) for n in KINDS}
        nmr = {n: sb(f"nmr_{n}", [P, KB]) for n in ("lny", "lnf")}

        p_max = [ps(f"p_max{j}", [P, L]) for j in range(2)]
        p_sc = [ps(f"p_sc{j}", [P, L]) for j in range(2)]
        p_lin = [ps(f"p_lin{j}", [P, L]) for j in range(2)]
        p_o = ps("p_o", [P, L])
        p_mt = ps("p_mt", [P, L])

        w_in, c_in = sem("w_in"), sem("c_in")
        consts, rows_set, w_split = sem("consts"), sem("rows_set"), sem("w_split")
        xa_in, xr_in = sem("xa_in"), sem("xr_in")
        stack_in = [sem(f"stack_in{p}") for p in range(PAIRS)]
        row_in = [sem(f"row_in{j}") for j in range(2)]
        stored = [sem(f"stored{j}") for j in range(2)]
        max_mm, red_done = sem("max_mm"), sem("red_done")
        sc_mm, exp_done = sem("sc_mm"), sem("exp_done")
        mt_mm, row_done = sem("mt_mm"), sem("row_done")
        pv_mm, ot_done = sem("pv_mm"), sem("ot_done")
        mm = {n: sem(f"mm_{n}") for n in LINEAR}
        hi_done = {n: sem(f"hi_{n}") for n in ("x1t", "x2t", "o2t", "qk")}
        ev = {n: sem(f"ev_{n}") for n in LINEAR}
        h_lo = sem("h_lo")
        den_done = sem("den_done")
        NS = {"ln1": KB, "lny": KB, "ln2": KB, "lnf": KB // 2}
        bn_done = {n: sem(f"s_bn_{n}") for n in KINDS}
        mv_done = {n: sem(f"s_mv_{n}") for n in KINDS}
        ve_done = {n: sem(f"s_ve_{n}") for n in KINDS}
        rstd_done = {n: sem(f"s_rstd_{n}") for n in KINDS}
        nmr_done = {n: sem(f"s_nmr_{n}") for n in ("lny", "lnf")}
        norm_done = {n: sem(f"s_norm_{n}") for n in KINDS}
        x1_done, x1_kept, final = sem("x1_done"), sem("x1_kept"), sem("final")
        block = ctx.enter_context(nc.Block())

        def there(b):
            return not isinstance(b, int) or 0 <= b < NB

        def above(b, k):
            return not isinstance(b, int) or b > 0 or k > 0

        def wait(eng, s, b, per, k):
            if isinstance(b, int):
                if b * per + k > 0:
                    eng.wait_ge(s, min(b * per + k, NB * per))
            else:
                eng.wait_ge(s, b * per + k)

        def unit_before(what, which, i):
            at = [j[:2] for j in UNITS].index((what, which)) - 2
            while True:
                name, n, off = UNITS[at % len(UNITS)]
                b = i + at // len(UNITS) + off
                if there(b):
                    return name, n, b
                at -= 2
                if isinstance(i, int) and i + at // len(UNITS) < -2:
                    return None

        def bank(what, which):
            return p_lin[[j[:2] for j in UNITS].index((what, which)) % 2]

        def steps(eng, step):
            for i in range(-AHEAD, BEHIND):
                step(i)
            with eng.Fori(BEHIND, NB - AHEAD) as i:
                step(i)
            for i in range(NB - AHEAD, NB + BEHIND):
                step(i)

        def prev(i, s, back):
            return (i, s - back) if s >= back else (i - 1, s - back + SLOTS)

        def two(ap, kb):
            return ap.rearrange("p (a n) -> p a n", n=P)[:, 0:kb + 1:kb, :]

        @block.sync
        def _(sp):
            for k in range(KD):
                sp.dma_start(probs[:, 0:8, :].rearrange("p a n -> p (a n)")[:, O_QKV + k * 3 * D:O_QKV + (k + 1) * 3 * D],
                             w_qkv_t[k * P:(k + 1) * P, :]).then_inc(w_in, 16)
                sp.dma_start(probs[:, 0:8, :].rearrange("p a n -> p (a n)")[:, O_W1 + k * F:O_W1 + (k + 1) * F],
                             w1[k * P:(k + 1) * P, :]).then_inc(w_in, 16)
                sp.dma_start(probs[:, 0:8, :].rearrange("p a n -> p (a n)")[:, O_WO + k * D:O_WO + (k + 1) * D],
                             w_out_t[k * P:(k + 1) * P, :]).then_inc(w_in, 16)
            w2_t = w2.rearrange("(h k p) n -> h p k n", p=P, k=KB)
            sp.dma_start(x1_old[:, :, :], w2_t[0]).then_inc(w_in, 16)
            sp.dma_start(yf[:, :, :], w2_t[1]).then_inc(w_in, 16)
            for dst, src in ((bqk_s, b_qk), (b1_s, b1), (bv_s, b_v), (bo_s, b_out), (b2_s, b2)):
                sp.dma_start(dst[:, :], src).then_inc(c_in, 16)

            def load_stack(b, p):
                t, r, buf = p // 4, 2 * HD * (p % 4), p % BUFS
                ready = b * 4 + 2 * t + 2
                if not isinstance(b, int):
                    ready = sp.to_reg(ready)
                wait(sp, sc_mm, b, PC, CH * (p - BUFS + 1))
                sp.wait_ge(ev["qk"], ready)
                for j in range(2):
                    rows = slice(r + j * HD, r + (j + 1) * HD)
                    for n in range(4):
                        a, c = n % 2, 2 + n // 2
                        sp.dma_start(stack[n * HD:(n + 1) * HD, buf, :, j, :].bitcast(F32),
                                     qk[rows, t, a:c + 1:c - a, :].bitcast(F32)).then_inc(stack_in[p], 16)

            def step(i):
                for s in range(SLOTS):
                    b, p = (i, s + 1) if s + 1 < SLOTS else (i + 1, 0)
                    if there(b):
                        load_stack(b, p)
                    b, p = prev(i, s, 1)
                    if there(b):
                        wait(sp, row_done, b, PAIRS, p + 1)
                        sp.dma_start(q_stack[MAXROW:K_ALL, p % BUFS, :, :].bitcast(F32),
                                     max_row[:, p % 2, :].unsqueeze(1).broadcast_to([2, 2, L]))\
                            .then_inc(row_in[p % 2], 16)

            steps(sp, step)

        @block.tensor
        def _(pe):
            pe.wait_ge(w_split, 4)
            pe.wait_ge(consts, 3)
            pe.wait_ge(rows_set, 3)

            def scores_for_max(i, s, c):
                buf, k = s % BUFS, CH * s + c
                if c == 0:
                    wait(pe, stack_in[s], i, 128, 128)
                wait(pe, red_done, i, PC, k - 1)
                dst = p_max[k % 2]
                if c < 2:
                    last = nc.tensor.matmul(dst[:, :], q_stack[0:MAXROW, buf, c, 0:P],
                                            k_stack[0:MAXROW, buf, c, :], start=True, stop=True)
                else:
                    kb = c - 1
                    for j in range(2):
                        last = nc.tensor.matmul(
                            dst[:, j * 2 * P:(j + 1) * 2 * P].rearrange("p (a n) -> p a n", a=2),
                            q_stack[0:MAXROW, buf, j, kb * P:(kb + 1) * P],
                            two(k_stack[0:MAXROW, buf, j, :], kb), start=True, stop=True)
                last.then_inc(max_mm, 1)

            def scores(i, s, c):
                b, p = prev(i, s, 2)
                if not there(b):
                    return
                buf, k = p % BUFS, CH * p + c
                if c == 0:
                    wait(pe, row_in[p % 2], b, 64, 16 * (p // 2 + 1))
                wait(pe, exp_done, b, PC, k - 1)
                dst = p_sc[k % 2]
                if c < 2:
                    last = nc.tensor.matmul(dst[:, :], k_stack[0:K_ALL, buf, c, 0:P],
                                            q_stack[0:K_ALL, buf, c, :], start=True, stop=True)
                else:
                    kb = c - 1
                    for j in range(2):
                        last = nc.tensor.matmul(
                            dst[:, j * 2 * P:(j + 1) * 2 * P].rearrange("p (a n) -> p a n", a=2),
                            k_stack[0:K_ALL, buf, j, kb * P:(kb + 1) * P],
                            two(q_stack[0:K_ALL, buf, j, :], kb), start=True, stop=True)
                last.then_inc(sc_mm, 1)

            def probs_x_values(i, s, kb):
                b, p = prev(i, s, 4)
                if not there(b):
                    return
                quad = p // 2
                wait(pe, exp_done, b, PC, CH * (2 * quad + 1) + max(kb + 1, 1) + 1)
                if kb == 0:
                    wait(pe, ev["v"], b, 2, 2)
                    wait(pe, ot_done, b, 4, quad)
                for j in range(4):
                    v = values[:, kb, 4 * quad + j, :]
                    o = p_o[VW * j:VW * (j + 1), :]
                    base = CH * (j // 2)
                    if kb == 0:
                        last = nc.tensor.matmul(o, v, probs[:, base + j % 2, :], start=True, stop=False,
                                                skip_group_check=True)
                    else:
                        last = nc.tensor.matmul(two(o, kb), v,
                                                probs[:, base + kb + 1, (j % 2) * 2 * P:(j % 2 + 1) * 2 * P]
                                                .rearrange("p (a n) -> p a n", a=2),
                                                start=False, stop=kb == KB - 1, skip_group_check=True)
                last.then_inc(pv_mm, 1)

            def transpose_max(i, s):
                b, p = prev(i, s, 1)
                if not there(b):
                    return
                wait(pe, red_done, b, PC, CH * (p + 1))
                wait(pe, row_done, b, PAIRS, p)
                for kb in range(KB):
                    last = nc.tensor.transpose(p_mt[0:2, kb * P:(kb + 1) * P],
                                               neg_max[:, p % 2, kb, :], ident[:, :])
                last.then_inc(mt_mm, 1)

            def transposed(dst, src, n):
                for kb in range(KB):
                    last = nc.tensor.transpose(dst[:, kb * P:(kb + 1) * P],
                                               src[:, kb, n * P:(n + 1) * P], ident[:, :])
                return last

            def product(dst, tiles, stationary, moving):
                for m, (a, c) in enumerate(PARTS):
                    for k in range(tiles):
                        last = nc.tensor.matmul(dst, stationary(a, k), moving(c, k),
                                                start=m == 0 and k == 0,
                                                stop=m == len(PARTS) - 1 and k == tiles - 1)
                return last

            def job(i, what, n, b):
                before = unit_before(what, n, i)
                if before:
                    wait(pe, ev[before[0]], before[2], LINEAR[before[0]], before[1] + 1)
                dst = bank(what, n)
                if what == "x1t":
                    wait(pe, norm_done["ln1"], b, 1, 1)
                    last = transposed(dst, xa, n)
                elif what == "x2t":
                    wait(pe, norm_done["ln2"], b, 1, 1)
                    last = transposed(dst, xh, n)
                elif what == "o2t":
                    wait(pe, ev["ot"], b, 4, 4)
                    last = transposed(dst, o_n, n)
                elif what == "ot":
                    wait(pe, ot_done, b, 4, n + 1)
                    for kb in range(KB):
                        last = nc.tensor.transpose(dst[:, kb * P:(kb + 1) * P],
                                                   o_t[:, kb * P:(kb + 1) * P], ident[:, :])
                elif what == "qk":
                    wait(pe, ev["x1t"], b, 2, 2)
                    col = O_QKV + (n % 2) * D + (n // 2) * P
                    last = product(dst[:, :], KD,
                                   lambda a, k: w_parts[a][:, col + k * 3 * D:col + k * 3 * D + P],
                                   lambda c, k: x1_t[c][:, k, :])
                elif what == "v":
                    for u in range(2):
                        kb = 2 * n + u
                        last = product(dst[:, u * D:(u + 1) * D], KD,
                                       lambda a, k: x1_t[a][:, k, kb * P:(kb + 1) * P],
                                       lambda c, k: w_parts[c][:, O_QKV + k * 3 * D + 2 * D:O_QKV + (k + 1) * 3 * D])
                elif what == "op":
                    wait(pe, ev["o2t"], b, 2, 2)
                    for u in range(2):
                        kb = 2 * n + u
                        last = product(dst[:, u * D:(u + 1) * D], KD,
                                       lambda a, k: o2_t[a][:, k, kb * P:(kb + 1) * P],
                                       lambda c, k: w_parts[c][:, O_WO + k * D:O_WO + (k + 1) * D])
                elif what == "f1":
                    wait(pe, ev["x2t"], b, 2, 2)
                    half = n // 4
                    for u in range(2):
                        col = O_W1 + (2 * (n % 4) + u) * P
                        last = product(dst[:, u * HALF:(u + 1) * HALF], KD,
                                       lambda a, k: w_parts[a][:, col + k * F:col + k * F + P],
                                       lambda c, k: x2_t[c][:, k, half * HALF:(half + 1) * HALF])
                elif what == "f2":
                    half, at = n // 2, (n % 2) * P
                    for k in range(KF):
                        if k % 2 == 0:
                            wait(pe, h_lo, b, 8, 4 * half + k // 2 + 1)
                        for m, (a, c) in enumerate(PARTS):
                            last = nc.tensor.matmul(dst[:, 0:D], h_parts[a][:, k, at:at + P],
                                                    w_parts[c][:, O_W2 + k * D:O_W2 + (k + 1) * D],
                                                    start=k == 0 and m == 0,
                                                    stop=k == KF - 1 and m == len(PARTS) - 1)
                last.then_inc(mm[what], 1)

            def step(i):
                for s in range(SLOTS):
                    for t in range(TURNS):
                        if there(i):
                            scores_for_max(i, s, t)
                        scores(i, s, t)
                        if s % 2 == 0 and t < KB:
                            probs_x_values(i, s, t)
                        if t == 0:
                            transpose_max(i, s)
                        for what, n, off in SCHEDULE.get((s, t), []):
                            if what in LINEAR and there(i + off):
                                job(i, what, n, i + off)

            steps(pe, step)

        @block.scalar
        def _(act):
            act.wait_ge(c_in, 80)
            act.wait_ge(w_split, 4)

            def exponentials(i, s, c):
                b, p = prev(i, s, 2)
                if not there(b):
                    return
                k, kb = CH * p + c, max(c - 1, 0)
                wait(act, sc_mm, b, PC, k + 1)
                wait(act, pv_mm, b, QC, 4 * (p // 2 - 1) + kb + 1)
                nc.scalar.activation(probs[:, CH * (p % 2) + c, :], p_sc[k % 2][:, :], ACT.Exp,
                                     scale=SCALE).then_inc(exp_done, 1)

            def read_output(i, s):
                b, p = prev(i, s, 4)
                if not there(b):
                    return
                quad = p // 2
                wait(act, pv_mm, b, QC, 4 * quad + 4)
                wait(act, mm["ot"], b, 4, quad)
                nc.scalar.activation(o_t[:, :], p_o[:, :], ACT.Copy).then_inc(ot_done, 1)

            def job(what, n, b):
                src = bank(what, n) if what in LINEAR else None
                if what in ("x1t", "x2t", "o2t"):
                    dst, reader, per = {"x1t": (x1_t, "v", 2), "x2t": (x2_t, "f1", 8),
                                        "o2t": (o2_t, "op", 2)}[what]
                    wait(act, mm[what], b, 2, n + 1)
                    wait(act, mm[reader], b, per, 0)
                    if what == "x1t":
                        wait(act, mm["qk"], b, 4, 0)
                    nc.scalar.activation(dst[0][:, n, :], src[:, :], ACT.Copy).then_inc(hi_done[what], 1)
                elif what == "qk":
                    wait(act, mm["qk"], b, 4, n + 1)
                    if n % 2 == 0:
                        for p in range(4 * (n // 2), 4 * (n // 2) + 4):
                            wait(act, stack_in[p], b, 128, 0)
                    nc.scalar.activation(qk[:, n // 2, 2 * (n % 2), :], src[:, :], ACT.Identity,
                                         bias=bqk_s[:, n:n + 1]).then_inc(hi_done["qk"], 1)
                elif what == "f1":
                    half = n // 4
                    wait(act, mm["f1"], b, 8, n + 1)
                    wait(act, h_lo, b, 8, n - 1)
                    wait(act, mm["f2"], b, 4, 2 * half)
                    for u in range(2):
                        m = 2 * (n % 4) + u
                        for dst in (h_f[:, n % 2, u, :], h_parts[0][:, m, :]):
                            last = nc.scalar.activation(dst, src[:, u * HALF:(u + 1) * HALF], ACT.Relu,
                                                        bias=b1_s[:, m:m + 1])
                    last.then_inc(ev["f1"], 1)
                elif what == "x1_keep":
                    wait(act, norm_done["ln2"], b, 1, 1)
                    wait(act, final, b, 2, 0)
                    nc.scalar.activation(x1_old[:, :, :], xr[:, :, :], ACT.Copy).then_inc(x1_kept, 1)
                elif what == "load_xr":
                    wait(act, x1_kept, b - 1, 1, 1)
                    act.dma_start(xr[:, :, :], x_t[b]).then_inc(xr_in, 16)
                elif what == "load_xa":
                    wait(act, mm["x1t"], b - 1, 2, 2)
                    act.dma_start(xa[:, :, :], x_t[b]).then_inc(xa_in, 16)
                elif what == "store":
                    wait(act, final, b, 2, n + 1)
                    act.dma_start(out_t[b, :, 2 * n:2 * n + 2, :],
                                  yf[:, 2 * n:2 * n + 2, :]).then_inc(stored[n], 16)
                elif what in ("lny_apply", "lnf_apply"):
                    kind = what[:3]
                    nb, y = NS[kind], {"lny": ya, "lnf": yf}[kind]
                    wait(act, nmr_done[kind], b, KB // nb, n + 1)
                    for kb in range(nb * n, nb * (n + 1)):
                        last = nc.scalar.activation(y[:, kb, :], y[:, kb, :], ACT.Identity,
                                                    bias=nmr[kind][:, kb:kb + 1],
                                                    scale=rstd[kind][:, kb:kb + 1])
                    last.then_inc(norm_done[kind], 1)

            def step(i):
                for s in range(SLOTS):
                    for t in range(TURNS):
                        exponentials(i, s, t)
                        if s % 2 == 0 and t == KB:
                            read_output(i, s)
                        for what, n, off in SCHEDULE.get((s, t), []):
                            if there(i + off):
                                job(what, n, i + off)

            steps(act, step)
            for n in range(2):
                act.wait_ge(stored[n], 16 * NB)

        @block.vector
        def _(dve):
            nc.vector.memset(stack[STACK:P, :, :, :, :].bitcast(F32), 0.0).then_inc(rows_set, 1)
            dve.wait_ge(rows_set, 1)
            nc.vector.memset(k_stack[MAXROW:MAXROW + 1, :, 0, :].bitcast(F32), 1.0)
            nc.vector.memset(k_stack[MAXROW:K_ALL, :, 1, :].bitcast(F32), 1.0).then_inc(rows_set, 1)
            dve.wait_ge(rows_set, 2)
            nc.vector.memset(k_stack[MAXROW:MAXROW + 1, :, 1, :].bitcast(F32), 0.0).then_inc(rows_set, 1)
            dve.wait_ge(w_in, 16 * (3 * KD + 2))
            w_src = ((0, O_W2, probs[:, 0:8, :].rearrange("p a n -> p (a n)")),
                     (O_W2, O_W2 + KB * D, x1_old[:, :, :].rearrange("p a n -> p (a n)")),
                     (O_W2 + KB * D, WCOLS, yf[:, :, :].rearrange("p a n -> p (a n)")))
            for lo, hi, src in w_src:
                nc.vector.tensor_copy(w_hi[:, lo:hi], src[:, 0:hi - lo]).then_inc(w_split, 1)
            dve.wait_ge(w_split, 3)
            for lo, hi, src in w_src:
                last = nc.vector.tensor_tensor(w_lo[:, lo:hi], src[:, 0:hi - lo],
                                               w_hi[:, lo:hi].bitcast(F32), ALU.subtract)
            last.then_inc(w_split, 1)
            dve.wait_ge(c_in, 80)
            dve.wait_ge(consts, 2)

            def maxima(i, s, c):
                k, j = CH * s + c, s % 2
                wait(dve, max_mm, i, PC, k + 1)
                if c == 0:
                    wait(dve, mt_mm, i, PAIRS, s - 1)
                if c < 2:
                    dst, src = neg_max[:, j, 0, c:c + 1], p_max[k % 2][:, :]
                else:
                    dst = neg_max[:, j, c - 1, :]
                    src = p_max[k % 2][:, :].rearrange("p (a n) -> p a n", a=2)
                nc.vector.tensor_reduce(dst, src, axis=AX.X, op=ALU.max, negate=True).then_inc(red_done, 1)

            def read_max(i, s):
                b, p = prev(i, s, 1)
                if not there(b):
                    return
                wait(dve, mt_mm, b, PAIRS, p + 1)
                wait(dve, row_in[p % 2], b, 64, 16 * (p // 2))
                nc.vector.tensor_copy(max_row[:, p % 2, :].bitcast(F32R), p_mt[0:2, :]).then_inc(row_done, 1)

            def stats(kind, src, n, b):
                nb = NS[kind]
                for kb in range(nb * n, nb * (n + 1)):
                    last = nc.vector.bn_stats(bn[kind][:, kb, :], src[:, kb, :])
                last.then_inc(bn_done[kind], 1)

            def mean_variance(kind, n, b):
                nb = NS[kind]
                for kb in range(nb * n, nb * (n + 1)):
                    last = nc.vector.bn_aggr(mv[kind][:, kb, :], bn[kind][:, kb, :])
                last.then_inc(mv_done[kind], 1)

            def minus_mean(kind, n, b):
                nb = NS[kind]
                wait(dve, rstd_done[kind], b, KB // nb, n + 1)
                at = slice(nb * n, nb * (n + 1))
                nc.vector.scalar_tensor_tensor(nmr[kind][:, at], mv[kind][:, at, 0], -1.0,
                                               rstd[kind][:, at], ALU.mult, ALU.mult)\
                    .then_inc(nmr_done[kind], 1)

            def normalise(kind, dst, src, b):
                wait(dve, rstd_done[kind], b, 1, 1)
                for kb in range(KB):
                    last = nc.vector.tensor_scalar(dst[:, kb, :], src[:, kb, :], mv[kind][:, kb, 0:1],
                                                   rstd[kind][:, kb:kb + 1], ALU.subtract, ALU.mult)
                last.then_inc(norm_done[kind], 1)

            def job(what, n, b):
                src = bank(what, n) if what in LINEAR else None
                if what in ("x1t", "x2t", "o2t"):
                    parts = {"x1t": x1_t, "x2t": x2_t, "o2t": o2_t}[what]
                    wait(dve, hi_done[what], b, 2, n + 1)
                    nc.vector.tensor_tensor(parts[1][:, n, :], src[:, :], parts[0][:, n, :].bitcast(F32),
                                            ALU.subtract).then_inc(ev[what], 1)
                elif what == "qk":
                    wait(dve, hi_done["qk"], b, 4, n + 1)
                    nc.vector.scalar_tensor_tensor(qk[:, n // 2, 2 * (n % 2) + 1, :], src[:, :], bqk_s[:, n:n + 1],
                                                   qk[:, n // 2, 2 * (n % 2), :].bitcast(F32), ALU.add, ALU.subtract)\
                        .then_inc(ev["qk"], 1)
                elif what == "v":
                    wait(dve, mm["v"], b, 2, n + 1)
                    wait(dve, pv_mm, b, QC, 0)
                    for u in range(2):
                        last = nc.vector.tensor_tensor(
                            values[:, 2 * n + u, :, 0:HD],
                            src[:, u * D:(u + 1) * D].rearrange("p (h d) -> p h d", d=HD),
                            bv_s[:, :].rearrange("p (h d) -> p h d", d=HD), ALU.add)
                    last.then_inc(ev["v"], 1)
                elif what == "ot":
                    wait(dve, mm["ot"], b, 4, n + 1)
                    wait(dve, mm["o2t"], b, 2, 0)
                    sums = src[:, :].rearrange("p (k h c) -> p k h c", k=KB, c=VW)
                    nc.vector.reciprocal(den[:, :, :], sums[:, :, :, HD]).then_inc(den_done, 1)
                    wait(dve, den_done, b, 4, n + 1)
                    nc.vector.tensor_tensor(
                        o_n[:, :, n * 4 * HD:(n + 1) * 4 * HD].rearrange("p k (h d) -> p k h d", d=HD),
                        sums[:, :, :, 0:HD],
                        den[:, :, :].unsqueeze(3).broadcast_to([P, KB, 4, HD]), ALU.mult)\
                        .then_inc(ev["ot"], 1)
                elif what == "op":
                    wait(dve, mm["op"], b, 2, n + 1)
                    wait(dve, x1_done, b, 1, 0)
                    for u in range(2):
                        last = nc.vector.tensor_tensor(ya[:, 2 * n + u, :], src[:, u * D:(u + 1) * D],
                                                       bo_s[:, :], ALU.add)
                    last.then_inc(ev["op"], 1)
                elif what == "f2":
                    wait(dve, mm["f2"], b, 4, n + 1)
                    wait(dve, stored[n // 2], b, 16, 0)
                    nc.vector.tensor_tensor(yf[:, n, :], src[:, 0:D], b2_s[:, :], ALU.add)\
                        .then_inc(ev["f2"], 1)
                elif what.endswith("_mean"):
                    mean_variance(what[:3], n, b)
                elif what == "ln1_stats":
                    wait(dve, xa_in, b, 16, 16)
                    stats("ln1", xa, 0, b)
                elif what == "ln1_apply":
                    normalise("ln1", xa, xa, b)
                elif what == "lny_stats":
                    wait(dve, ev["op"], b, 2, 2)
                    stats("lny", ya, 0, b)
                elif what == "lny_apply":
                    minus_mean("lny", 0, b)
                elif what == "ln2_stats":
                    wait(dve, x1_done, b, 1, 1)
                    stats("ln2", xr, 0, b)
                elif what == "ln2_apply":
                    wait(dve, mm["x2t"], b, 2, 0)
                    normalise("ln2", xh, xr, b)
                elif what == "lnf_stats":
                    wait(dve, ev["f2"], b, 4, 2 * n + 2)
                    stats("lnf", yf, n, b)
                elif what == "lnf_apply":
                    minus_mean("lnf", n, b)

            def step(i):
                for s in range(SLOTS):
                    for t in range(TURNS):
                        for what, n, off in SCHEDULE.get((s, t), []):
                            if what.endswith("_mean") and there(i + off):
                                wait(dve, bn_done[what[:3]], i + off, KB // NS[what[:3]], n + 1)
                        if there(i):
                            maxima(i, s, t)
                        if t == 0:
                            read_max(i, s)
                        for what, n, off in SCHEDULE.get((s, t), []):
                            if there(i + off):
                                job(what, n, i + off)

            steps(dve, step)

        @block.gpsimd
        def _(pool):
            nc.gpsimd.memset(ident[:, :], 0.0).then_inc(consts, 1)
            nc.gpsimd.memset(minus_half[:, :], -0.5)
            nc.gpsimd.memset(eps[:, :], EPS)
            nc.gpsimd.memset(values[:, :, :, :], 1.0).then_inc(consts, 1)
            pool.wait_ge(consts, 2)
            nc.gpsimd.affine_select(out=ident[:, :], in_=ident[:, :], compare_op=ALU.not_equal, fill=1.0,
                                    base=0, pattern=[[-1, P]], channel_multiplier=1).then_inc(consts, 1)

            def one_over_std(kind, n, b):
                nb = NS[kind]
                at = slice(nb * n, nb * (n + 1))
                wait(pool, mv_done[kind], b, KB // nb, n + 1)
                nc.gpsimd.tensor_tensor(ve[kind][:, at], mv[kind][:, at, 1], eps[:, at], ALU.add)\
                    .then_inc(ve_done[kind], 1)
                wait(pool, ve_done[kind], b, KB // nb, n + 1)
                nc.gpsimd.tensor_tensor(rstd[kind][:, at], ve[kind][:, at], minus_half[:, at],
                                        ALU.pow).then_inc(rstd_done[kind], 1)

            def job(what, n, b):
                if what.endswith("_mean"):
                    one_over_std(what[:3], n, b)
                elif what == "f1":
                    wait(pool, ev["f1"], b, 8, n + 1)
                    for u in range(2):
                        m = 2 * (n % 4) + u
                        last = nc.gpsimd.tensor_tensor(h_parts[1][:, m, :], h_f[:, n % 2, u, :],
                                                       h_parts[0][:, m, :].bitcast(F32), ALU.subtract)
                    last.then_inc(h_lo, 1)
                elif what == "lny_apply":
                    wait(pool, xr_in, b, 16, 16)
                    wait(pool, norm_done["lny"], b, 1, 1)
                    nc.gpsimd.tensor_tensor(xr[:, :, :], xr[:, :, :], ya[:, :, :], ALU.add)\
                        .then_inc(x1_done, 1)
                elif what == "lnf_apply":
                    wait(pool, x1_kept, b, 1, 1)
                    wait(pool, norm_done["lnf"], b, 2, n + 1)
                    at = slice(2 * n, 2 * n + 2)
                    nc.gpsimd.tensor_tensor(yf[:, at, :], yf[:, at, :], x1_old[:, at, :], ALU.add)\
                        .then_inc(final, 1)

            def step(i):
                for s in range(SLOTS):
                    for t in range(TURNS):
                        for what, n, off in SCHEDULE.get((s, t), []):
                            if there(i + off):
                                job(what, n, i + off)

            steps(pool, step)


def kernel(L0_attn_x, L0_attn_w_qkv, L0_attn_b_qkv, L0_attn_w_out, L0_attn_b_out,
           L0_ffn_W1, L0_ffn_b1, L0_ffn_W2, L0_ffn_b2):
    import numpy as np
    import concourse.bacc as bacc
    from concourse.bass_utils import run_bass_kernel_spmd

    P = 128
    x = np.ascontiguousarray(L0_attn_x)
    D = x.shape[2]
    b_qkv, b1 = np.asarray(L0_attn_b_qkv), np.asarray(L0_ffn_b1)

    def rows(a):
        return np.ascontiguousarray(np.broadcast_to(np.asarray(a), (P, D)))

    b_qk = np.ascontiguousarray(b_qkv[:2 * D].reshape(2, D // P, P).transpose(2, 1, 0).reshape(P, 4))
    arrays = {
        "x": x,
        "w_qkv_t": np.ascontiguousarray(np.asarray(L0_attn_w_qkv).T),
        "b_qk": b_qk,
        "b_v": rows(b_qkv[2 * D:]),
        "w_out_t": np.ascontiguousarray(np.asarray(L0_attn_w_out).T),
        "b_out": rows(L0_attn_b_out),
        "w1": np.ascontiguousarray(L0_ffn_W1),
        "b1": np.ascontiguousarray(b1.reshape(-1, P).T),
        "w2": np.ascontiguousarray(L0_ffn_W2),
        "b2": rows(L0_ffn_b2),
    }
    nc = bacc.Bacc("TRN2", target_bir_lowering=False, num_devices=1)
    args = [nc.dram_tensor(name, a.shape, mybir.dt.from_np(a.dtype), kind="ExternalInput").ap()
            for name, a in arrays.items()]
    out = nc.dram_tensor("out", x.shape, mybir.dt.float32, kind="ExternalOutput").ap()
    sandwich(nc, *args, out)
    res = run_bass_kernel_spmd(nc, [arrays], core_ids=[0])
    return res.results[0]["out"]
```

```python
import concourse.bass as bass
from concourse import mybir
from contextlib import ExitStack

F32 = mybir.dt.float32
F32R = mybir.dt.float32r
ALU = mybir.AluOpType
ACT = mybir.ActivationFunctionType
AX = mybir.AxisListType

SCHEDULE = {
    (0, 0): [("mt", 7, -1), ("x2t", 1, -2), ("ln1_mean", 0, 1)],
    (0, 1): [("ln1_stats", 1, 1)],
    (0, 2): [("f2", 3, -3)],
    (0, 3): [("lnf_stats", 1, -3), ("ot", 2, -1)],
    (0, 4): [("lnf_mean", 1, -3), ("ln1_mean", 1, 1)],
    (1, 0): [("f1", 0, -2), ("mt", 0, 0), ("qk", 2, 0), ("lnf_apply", 1, -3)],
    (1, 1): [("ln1_apply", 0, 1), ("ln1_apply", 1, 1)],
    (1, 2): [("qk", 3, 0), ("x1_keep", 0, -2)],
    (1, 3): [("f1", 1, -2), ("x1_keep", 1, -2)],
    (1, 4): [("store", 1, -3)],
    (2, 0): [("mt", 1, 0), ("v", 0, 0)],
    (2, 1): [("load_xr", 0, -1), ("v", 1, 0)],
    (2, 2): [("ot", 3, -1), ("o2t", 0, -1)],
    (2, 4): [("o2t", 1, -1), ("f1", 2, -2)],
    (3, 0): [("mt", 2, 0)],
    (3, 1): [("f1", 3, -2)],
    (3, 3): [("op", 0, -1)],
    (3, 4): [("lny_stats", 0, -1)],
    (4, 0): [("mt", 3, 0)],
    (4, 1): [("x1t", 0, 1), ("op", 1, -1)],
    (4, 2): [("lny_mean", 0, -1), ("lny_stats", 1, -1), ("ot", 0, 0)],
    (4, 3): [("lny_mean", 1, -1), ("x1t", 1, 1), ("lny_apply", 0, -1)],
    (4, 4): [("f2", 0, -2), ("load_xa", 0, 2)],
    (5, 0): [("lny_apply", 1, -1), ("mt", 4, 0), ("ln2_stats", 0, -1), ("ln2_stats", 1, -1), ("qk", 0, 1)],
    (5, 2): [("qk", 1, 1), ("f2", 1, -2)],
    (5, 3): [("ln2_mean", 0, -1)],
    (6, 0): [("ln2_mean", 1, -1), ("mt", 5, 0), ("ln2_apply", 0, -1), ("lnf_stats", 0, -2)],
    (6, 1): [("f1", 4, -2), ("f1", 5, -2), ("lnf_mean", 0, -2), ("ot", 1, 0)],
    (6, 4): [("ln2_apply", 1, -1)],
    (7, 0): [("f1", 6, -2), ("mt", 6, 0)],
    (7, 2): [("lnf_apply", 0, -2), ("f1", 7, -2), ("x2t", 0, -1), ("store", 0, -2)],
    (7, 3): [("ln1_stats", 0, 2)],
    (7, 4): [("f2", 2, -2)],
}
SLOTS, TURNS = 8, 5
SC_TURN = 3
PV_TURNS = {2: (0, 1), 4: (2, 3)}
READ_TURN = 0
LINEAR = {"mt": 8, "x1t": 2, "x2t": 2, "o2t": 2, "qk": 4, "v": 2, "ot": 4, "op": 2, "f1": 8, "f2": 4}
UNITS = [job for s in range(SLOTS) for t in range(TURNS)
         for job in SCHEDULE.get((s, t), []) if job[0] in LINEAR]
AHEAD = 2
BEHIND = 3
LOOP_FROM = BEHIND + 1


def sandwich(nc, x, w_qkv_t, b_qk, b_v, w_out_t, b_out, w1, b1, w2, b2, ident_in, own_block_in,
             stack_rows_in, out):
    NB, L, D = x.shape
    P = 128
    KB = L // P
    H, HD = 16, 16
    PAIRS = H // 2
    F = w1.shape[1]
    KD, KF = D // P, F // P
    HALF = L // 2
    VW = 32
    STACK = 4 * HD
    MAXROW = STACK + 2 * KB
    K_ALL = MAXROW + 2 * KB
    BUFS = 4
    CH = 5
    PC, QC = CH * PAIRS, KB * KB
    EPS = 1e-5
    SCALE = float(HD) ** -0.5
    PARTS = ((0, 0), (0, 1), (1, 0))
    O_QKV, O_W1 = 0, KD * 3 * D
    O_WO = O_W1 + KD * F
    O_W2 = O_WO + KD * D
    WCOLS = O_W2 + KF * D
    LIN = 3
    assert PC % 2 == 0

    x_t = x.rearrange("b (k p) d -> b p k d", p=P)
    out_t = out.rearrange("b (k p) d -> b p k d", p=P)

    with ExitStack() as ctx:
        def sb(name, shape, dt=F32):
            return ctx.enter_context(nc.sbuf_tensor(name, shape, dt))

        def ps(name, shape):
            return ctx.enter_context(nc.psum_tensor(name, shape, F32))

        def sem(name):
            return ctx.enter_context(nc.semaphore(name))

        w_hi, w_lo = sb("w_hi", [P, WCOLS], F32R), sb("w_lo", [P, WCOLS], F32R)
        w_parts = (w_hi, w_lo)
        ident = sb("ident", [P, P])
        bqk_s, b1_s = sb("bqk_s", [P, 4]), sb("b1_s", [P, KF])
        bv_s, bo_s, b2_s = sb("bv_s", [P, D]), sb("bo_s", [P, D]), sb("b2_s", [P, D])
        minus_half, eps = sb("minus_half", [P, KB]), sb("eps", [P, KB])
        xa = sb("xa", [P, KB, D])
        x1_t = [sb(f"x1_{n}", [P, KD, L], F32R) for n in ("hi", "lo")]
        qk = sb("qk", [P, 2, 4, L], F32R)
        stack = sb("stack", [P, BUFS, 2, 2, L], F32R)
        q_stack, k_stack = stack[:, :, 0, :, :], stack[:, :, 1, :, :]
        neg_max = sb("neg_max", [P, 2, KB, 2])
        own_block = sb("own_block", [2 * KB, L])
        max_row = sb("max_row", [2 * KB, L])
        values = sb("values", [P, KB, H, VW])
        probs = sb("probs", [P, 2 * CH, L])
        o_t = sb("o_t", [P, L])
        den = sb("den", [P, KB, 4])
        o_n = sb("o_n", [P, KB, D])
        o2_t = [sb(f"o2_{n}", [P, KD, L], F32R) for n in ("hi", "lo")]
        ya = sb("ya", [P, KB, D])
        xr = sb("xr", [P, KB, D])
        xh = sb("xh", [P, KB, D])
        x2_t = [sb(f"x2_{n}", [P, KD, L], F32R) for n in ("hi", "lo")]
        x1_old = sb("x1_old", [P, KB, D])
        h_f = sb("h_f", [P, 2, 2, HALF])
        h_parts = [sb(f"h_{n}", [P, KF, HALF], F32R) for n in ("hi", "lo")]
        yf = sb("yf", [P, KB, D])
        KINDS = ("ln1", "lny", "ln2", "lnf")
        bn = {n: sb(f"bn_{n}", [P, KB, 6]) for n in KINDS}
        mv = {n: sb(f"mv_{n}", [P, KB, 2]) for n in KINDS}
        ve = {n: sb(f"ve_{n}", [P, KB]) for n in KINDS}
        rstd = {n: sb(f"rstd_{n}", [P, KB]) for n in KINDS}
        nmr = {n: sb(f"nmr_{n}", [P, KB]) for n in ("lny", "lnf")}

        p_max = [ps(f"p_max{j}", [P, L]) for j in range(2)]
        p_sc = [ps(f"p_sc{j}", [P, L]) for j in range(2)]
        p_lin = [ps(f"p_lin{j}", [P, L]) for j in range(LIN)]
        p_o = ps("p_o", [P, L])

        qkv_in, rest_in = sem("qkv_in"), sem("rest_in")
        hi_split, lo_split = sem("hi_split"), sem("lo_split")
        ident_set, c_in, rows_in = sem("ident_set"), sem("c_in"), sem("rows_in")
        rows_raw_in, rows_set = sem("rows_raw_in"), sem("rows_set")
        consts = sem("consts")
        xa_in, xr_in = sem("xa_in"), sem("xr_in")
        stack_in = [[sem(f"stack_in{p}_{j}") for j in range(2)] for p in range(PAIRS)]
        row_in = sem("row_in")
        stored = [sem(f"stored{j}") for j in range(2)]
        max_mm, red_done = sem("max_mm"), sem("red_done")
        sc_mm, exp_done = sem("sc_mm"), sem("exp_done")
        pv_mm, ot_done = sem("pv_mm"), sem("ot_done")
        mm = {n: sem(f"mm_{n}") for n in LINEAR}
        hi_done = {n: sem(f"hi_{n}") for n in ("x1t", "x2t", "o2t", "qk")}
        ev = {n: sem(f"ev_{n}") for n in LINEAR}
        h_lo = sem("h_lo")
        den_done = sem("den_done")
        HB = KB // 2
        bn_done = {n: sem(f"s_bn_{n}") for n in KINDS}
        mv_done = {n: sem(f"s_mv_{n}") for n in KINDS}
        ve_done = {n: sem(f"s_ve_{n}") for n in KINDS}
        rstd_done = {n: sem(f"s_rstd_{n}") for n in KINDS}
        nmr_done = {n: sem(f"s_nmr_{n}") for n in ("lny", "lnf")}
        norm_done = {n: sem(f"s_norm_{n}") for n in KINDS}
        x1_done, x1_kept, final = sem("x1_done"), sem("x1_kept"), sem("final")
        block = ctx.enter_context(nc.Block())

        w_stage = probs[:, :, :].rearrange("p a n -> p (a n)")
        rows_raw = h_f[0:K_ALL - STACK, :, :, :].rearrange("r a u n -> r (a u n)")
        rows_f32r = ya[0:K_ALL - STACK, :, :].rearrange("r k n -> r (k n)")
        W_REST = ((O_W1, O_W2, w_stage[:, O_W1:O_W2]),
                  (O_W2, O_W2 + KB * D, x1_old[:, :, :].rearrange("p a n -> p (a n)")),
                  (O_W2 + KB * D, WCOLS, yf[:, :, :].rearrange("p a n -> p (a n)")))

        def there(b):
            return not isinstance(b, int) or 0 <= b < NB

        def above(b, k):
            return not isinstance(b, int) or b > 0 or k > 0

        def wait(eng, s, b, per, k):
            if isinstance(b, int):
                if b * per + k > 0:
                    eng.wait_ge(s, min(b * per + k, NB * per))
            else:
                eng.wait_ge(s, b * per + k)

        def place(what, which):
            return [job[:2] for job in UNITS].index((what, which))

        def bank_of(at):
            return at % len(UNITS) % LIN

        def unit_before(what, which, i):
            mine = place(what, which)
            for at in range(mine - 1, -4 * len(UNITS), -1):
                name, n, off = UNITS[at % len(UNITS)]
                b = i + at // len(UNITS) + off
                if bank_of(at) == bank_of(mine) and there(b):
                    return name, n, b
            return None

        def bank(what, which):
            return p_lin[bank_of(place(what, which))]

        def steps(eng, step, setup):
            for i in range(-AHEAD, LOOP_FROM):
                setup(i)
                step(i)
            with eng.Fori(LOOP_FROM, NB - AHEAD) as i:
                step(i)
            for i in range(NB - AHEAD, NB + BEHIND):
                step(i)

        def prev(i, s, back):
            return (i, s - back) if s >= back else (i - 1, s - back + SLOTS)

        def second(i, s, t):
            return prev(i, s, 1) + (t - SC_TURN,) if t >= SC_TURN else prev(i, s, 2) + (t + TURNS - SC_TURN,)

        def two(ap, kb):
            return ap.rearrange("p (a n) -> p a n", n=P)[:, 0:kb + 1:kb, :]

        @block.sync
        def _(sp):
            sp.dma_start(ident[:, :], ident_in).then_inc(ident_set, 16)
            for k in range(KD):
                sp.dma_start(w_stage[:, O_QKV + k * 3 * D:O_QKV + (k + 1) * 3 * D],
                             w_qkv_t[k * P:(k + 1) * P, :]).then_inc(qkv_in, 16)
            sp.dma_start(rows_raw, stack_rows_in).then_inc(rows_raw_in, 16)
            for dst, src in ((bqk_s, b_qk), (bv_s, b_v), (own_block, own_block_in), (bo_s, b_out),
                             (b1_s, b1), (b2_s, b2)):
                sp.dma_start(dst[:, :], src).then_inc(c_in, 16)
            for k in range(KD):
                sp.dma_start(w_stage[:, O_W1 + k * F:O_W1 + (k + 1) * F],
                             w1[k * P:(k + 1) * P, :]).then_inc(rest_in, 16)
                sp.dma_start(w_stage[:, O_WO + k * D:O_WO + (k + 1) * D],
                             w_out_t[k * P:(k + 1) * P, :]).then_inc(rest_in, 16)
            w2_t = w2.rearrange("(h k p) n -> h p k n", p=P, k=KB)
            sp.dma_start(x1_old[:, :, :], w2_t[0]).then_inc(rest_in, 16)
            sp.dma_start(yf[:, :, :], w2_t[1]).then_inc(rest_in, 16)
            sp.wait_ge(rows_set, 1)
            sp.dma_start(stack[STACK:MAXROW, :, 0, :, :].bitcast(F32).rearrange("r b j n -> r b (j n)"),
                         rows_f32r[0:MAXROW - STACK, :].unsqueeze(1)
                         .broadcast_to([MAXROW - STACK, BUFS, 2 * L])).then_inc(rows_in, 16)
            sp.dma_start(stack[STACK:K_ALL, :, 1, :, :].bitcast(F32).rearrange("r b j n -> r b (j n)"),
                         rows_f32r.unsqueeze(1).broadcast_to([K_ALL - STACK, BUFS, 2 * L]))\
                .then_inc(rows_in, 16)

            def load_stack(b, p):
                t, r, buf = p // 4, 2 * HD * (p % 4), p % BUFS
                ready = b * 4 + 2 * t + 2
                if not isinstance(b, int):
                    ready = sp.to_reg(ready)
                wait(sp, sc_mm, b, PC, CH * (p - BUFS + 1))
                sp.wait_ge(ev["qk"], ready)
                for j in range(2):
                    rows = slice(r + j * HD, r + (j + 1) * HD)
                    for n in range(4):
                        a, c = n % 2, 2 + n // 2
                        sp.dma_start(stack[n * HD:(n + 1) * HD, buf, :, j, :].bitcast(F32),
                                     qk[rows, t, a:c + 1:c - a, :].bitcast(F32)).then_inc(stack_in[p][j], 16)

            def step(i):
                for s in range(SLOTS):
                    b, p = prev(i, s, 1)
                    if there(b):
                        wait(sp, ev["mt"], b, PAIRS, p + 1)
                        sp.dma_start(q_stack[MAXROW:K_ALL, p % BUFS, :, :].bitcast(F32),
                                     max_row[:, :].unsqueeze(1).broadcast_to([2 * KB, 2, L]))\
                            .then_inc(row_in, 16)
                    b, p = (i, s + 2) if s + 2 < SLOTS else (i + 1, s + 2 - SLOTS)
                    if there(b):
                        load_stack(b, p)

            steps(sp, step, lambda i: None)

        @block.tensor
        def _(pe):
            def setup(i):
                if i == -1:
                    pe.wait_ge(ident_set, 16)
                elif i == 0:
                    pe.wait_ge(rows_in, 32)
                    pe.wait_ge(consts, 2)
                elif i == 1:
                    pe.wait_ge(lo_split, 3)

            def scores_for_max(i, s, c):
                buf, k = s % BUFS, CH * s + c
                if c < 2:
                    wait(pe, stack_in[s][c], i, 64, 64)
                wait(pe, red_done, i, PC, k - 1)
                dst = p_max[k % 2]
                if c < 2:
                    last = nc.tensor.matmul(dst[:, :], q_stack[0:MAXROW, buf, c, 0:P],
                                            k_stack[0:MAXROW, buf, c, :], start=True, stop=True)
                else:
                    kb = c - 1
                    for j in range(2):
                        last = nc.tensor.matmul(
                            dst[:, j * 2 * P:(j + 1) * 2 * P].rearrange("p (a n) -> p a n", a=2),
                            q_stack[0:MAXROW, buf, j, kb * P:(kb + 1) * P],
                            two(k_stack[0:MAXROW, buf, j, :], kb), start=True, stop=True)
                last.then_inc(max_mm, 1)

            def scores(i, s, t):
                b, p, c = second(i, s, t)
                if not there(b):
                    return
                buf, k = p % BUFS, CH * p + c
                if c == 0:
                    wait(pe, row_in, b, 128, 16 * (p + 1))
                wait(pe, exp_done, b, PC, k - 1)
                dst = p_sc[k % 2]
                if c < 2:
                    last = nc.tensor.matmul(dst[:, :], k_stack[0:K_ALL, buf, c, 0:P],
                                            q_stack[0:K_ALL, buf, c, :], start=True, stop=True)
                else:
                    kb = c - 1
                    for j in range(2):
                        last = nc.tensor.matmul(
                            dst[:, j * 2 * P:(j + 1) * 2 * P].rearrange("p (a n) -> p a n", a=2),
                            k_stack[0:K_ALL, buf, j, kb * P:(kb + 1) * P],
                            two(q_stack[0:K_ALL, buf, j, :], kb), start=True, stop=True)
                last.then_inc(sc_mm, 1)

            def probs_x_values(i, s, kb):
                b, p = prev(i, s, 2)
                if not there(b):
                    return
                quad = p // 2
                wait(pe, exp_done, b, PC, CH * (2 * quad + 1) + max(kb + 1, 1) + 1)
                if kb == 0:
                    wait(pe, ev["v"], b, 2, 2)
                    wait(pe, ot_done, b, 4, quad)
                for j in range(4):
                    v = values[:, kb, 4 * quad + j, :]
                    o = p_o[VW * j:VW * (j + 1), :]
                    base = CH * (j // 2)
                    if kb == 0:
                        last = nc.tensor.matmul(o, v, probs[:, base + j % 2, :], start=True, stop=False,
                                                skip_group_check=True)
                    else:
                        last = nc.tensor.matmul(two(o, kb), v,
                                                probs[:, base + kb + 1, (j % 2) * 2 * P:(j % 2 + 1) * 2 * P]
                                                .rearrange("p (a n) -> p a n", a=2),
                                                start=False, stop=kb == KB - 1, skip_group_check=True)
                last.then_inc(pv_mm, 1)

            def transposed(dst, src, n):
                for kb in range(KB):
                    last = nc.tensor.transpose(dst[:, kb * P:(kb + 1) * P],
                                               src[:, kb, n * P:(n + 1) * P], ident[:, :])
                return last

            def product(dst, tiles, stationary, moving):
                for m, (a, c) in enumerate(PARTS):
                    for k in range(tiles):
                        last = nc.tensor.matmul(dst, stationary(a, k), moving(c, k),
                                                start=m == 0 and k == 0,
                                                stop=m == len(PARTS) - 1 and k == tiles - 1)
                return last

            def job(i, what, n, b):
                before = unit_before(what, n, i)
                if before:
                    wait(pe, ev[before[0]], before[2], LINEAR[before[0]], before[1] + 1)
                dst = bank(what, n)
                if what == "mt":
                    wait(pe, red_done, b, PC, CH * (n + 1))
                    last = nc.tensor.transpose(dst[0:2 * KB, 0:P],
                                               neg_max[:, n % 2, :, :].rearrange("p k h -> p (k h)"),
                                               ident[:, :])
                elif what == "x1t":
                    wait(pe, norm_done["ln1"], b, 2, 2)
                    last = transposed(dst, xa, n)
                elif what == "x2t":
                    wait(pe, norm_done["ln2"], b, 2, 2)
                    last = transposed(dst, xh, n)
                elif what == "o2t":
                    wait(pe, ev["ot"], b, 4, 2 * n + 2)
                    last = transposed(dst, o_n, n)
                elif what == "ot":
                    wait(pe, ot_done, b, 4, n + 1)
                    for kb in range(KB):
                        last = nc.tensor.transpose(dst[:, kb * P:(kb + 1) * P],
                                                   o_t[:, kb * P:(kb + 1) * P], ident[:, :])
                elif what == "qk":
                    if isinstance(b, int) and (n, b) == (0, 0):
                        pe.wait_ge(lo_split, 1)
                    wait(pe, ev["x1t"], b, 2, 2)
                    col = O_QKV + (n % 2) * D + (n // 2) * P
                    last = product(dst[:, :], KD,
                                   lambda a, k: w_parts[a][:, col + k * 3 * D:col + k * 3 * D + P],
                                   lambda c, k: x1_t[c][:, k, :])
                elif what == "v":
                    for u in range(2):
                        kb = 2 * n + u
                        last = product(dst[:, u * D:(u + 1) * D], KD,
                                       lambda a, k: x1_t[a][:, k, kb * P:(kb + 1) * P],
                                       lambda c, k: w_parts[c][:, O_QKV + k * 3 * D + 2 * D:O_QKV + (k + 1) * 3 * D])
                elif what == "op":
                    wait(pe, ev["o2t"], b, 2, 2)
                    for u in range(2):
                        kb = 2 * n + u
                        last = product(dst[:, u * D:(u + 1) * D], KD,
                                       lambda a, k: o2_t[a][:, k, kb * P:(kb + 1) * P],
                                       lambda c, k: w_parts[c][:, O_WO + k * D:O_WO + (k + 1) * D])
                elif what == "f1":
                    wait(pe, ev["x2t"], b, 2, 2)
                    half = n // 4
                    for u in range(2):
                        col = O_W1 + (2 * (n % 4) + u) * P
                        last = product(dst[:, u * HALF:(u + 1) * HALF], KD,
                                       lambda a, k: w_parts[a][:, col + k * F:col + k * F + P],
                                       lambda c, k: x2_t[c][:, k, half * HALF:(half + 1) * HALF])
                elif what == "f2":
                    half, at = n // 2, (n % 2) * P
                    for k in range(KF):
                        if k % 2 == 0:
                            wait(pe, h_lo, b, 8, 4 * half + k // 2 + 1)
                        for m, (a, c) in enumerate(PARTS):
                            last = nc.tensor.matmul(dst[:, 0:D], h_parts[a][:, k, at:at + P],
                                                    w_parts[c][:, O_W2 + k * D:O_W2 + (k + 1) * D],
                                                    start=k == 0 and m == 0,
                                                    stop=k == KF - 1 and m == len(PARTS) - 1)
                last.then_inc(mm[what], 1)

            def step(i):
                for s in range(SLOTS):
                    for t in range(TURNS):
                        if there(i):
                            scores_for_max(i, s, t)
                        scores(i, s, t)
                        for what, n, off in SCHEDULE.get((s, t), []):
                            if what in LINEAR and there(i + off):
                                job(i, what, n, i + off)
                        for kb in PV_TURNS.get(t, ()) if s % 2 == 1 else ():
                            probs_x_values(i, s, kb)

            steps(pe, step, setup)

        @block.scalar
        def _(act):
            def setup(i):
                if i == -1:
                    act.wait_ge(qkv_in, 16 * KD)
                    nc.scalar.activation(w_hi[:, 0:O_W1], w_stage[:, 0:O_W1], ACT.Copy).then_inc(hi_split, 1)
                    act.wait_ge(c_in, 96)
                elif i == 0:
                    act.wait_ge(rest_in, 16 * (2 * KD + 2))
                    for lo, hi, src in W_REST:
                        nc.scalar.activation(w_hi[:, lo:hi], src, ACT.Copy).then_inc(hi_split, 1)
                    act.wait_ge(lo_split, 3)

            def exponentials(i, s, t):
                b, p, c = second(i, s, t)
                if not there(b):
                    return
                k, kb = CH * p + c, max(c - 1, 0)
                wait(act, sc_mm, b, PC, k + 1)
                wait(act, pv_mm, b, QC, 4 * (p // 2 - 1) + kb + 1)
                nc.scalar.activation(probs[:, CH * (p % 2) + c, :], p_sc[k % 2][:, :], ACT.Exp,
                                     scale=SCALE).then_inc(exp_done, 1)

            def read_output(i, s):
                b, p = prev(i, s, 3)
                if not there(b):
                    return
                quad = p // 2
                wait(act, pv_mm, b, QC, 4 * quad + 4)
                wait(act, mm["ot"], b, 4, quad)
                nc.scalar.activation(o_t[:, :], p_o[:, :], ACT.Copy).then_inc(ot_done, 1)

            def job(what, n, b):
                src = bank(what, n) if what in LINEAR else None
                if what in ("x1t", "x2t", "o2t"):
                    dst, reader, per = {"x1t": (x1_t, "v", 2), "x2t": (x2_t, "f1", 8),
                                        "o2t": (o2_t, "op", 2)}[what]
                    wait(act, mm[what], b, 2, n + 1)
                    wait(act, mm[reader], b, per, 0)
                    if what == "x1t":
                        wait(act, mm["qk"], b, 4, 0)
                    nc.scalar.activation(dst[0][:, n, :], src[:, :], ACT.Copy).then_inc(hi_done[what], 1)
                elif what == "qk":
                    wait(act, mm["qk"], b, 4, n + 1)
                    if n % 2 == 0:
                        for p in range(4 * (n // 2), 4 * (n // 2) + 4):
                            for j in range(2):
                                wait(act, stack_in[p][j], b, 64, 0)
                    nc.scalar.activation(qk[:, n // 2, 2 * (n % 2), :], src[:, :], ACT.Identity,
                                         bias=bqk_s[:, n:n + 1]).then_inc(hi_done["qk"], 1)
                elif what == "f1":
                    half = n // 4
                    wait(act, mm["f1"], b, 8, n + 1)
                    wait(act, h_lo, b, 8, n - 1)
                    wait(act, mm["f2"], b, 4, 2 * half)
                    for u in range(2):
                        m = 2 * (n % 4) + u
                        for dst in (h_f[:, n % 2, u, :], h_parts[0][:, m, :]):
                            last = nc.scalar.activation(dst, src[:, u * HALF:(u + 1) * HALF], ACT.Relu,
                                                        bias=b1_s[:, m:m + 1])
                    last.then_inc(ev["f1"], 1)
                elif what == "x1_keep":
                    at = slice(HB * n, HB * (n + 1))
                    wait(act, norm_done["ln2"], b, 2, n + 1)
                    wait(act, final, b - 1, 2, n + 1)
                    nc.scalar.activation(x1_old[:, at, :], xr[:, at, :], ACT.Copy).then_inc(x1_kept, 1)
                elif what == "load_xr":
                    wait(act, x1_kept, b - 1, 2, 2)
                    act.dma_start(xr[:, :, :], x_t[b]).then_inc(xr_in, 16)
                elif what == "load_xa":
                    wait(act, mm["x1t"], b - 1, 2, 2)
                    act.dma_start(xa[:, :, :], x_t[b]).then_inc(xa_in, 16)
                elif what == "store":
                    wait(act, final, b, 2, n + 1)
                    act.dma_start(out_t[b, :, 2 * n:2 * n + 2, :],
                                  yf[:, 2 * n:2 * n + 2, :]).then_inc(stored[n], 16)
                elif what in ("lny_apply", "lnf_apply"):
                    kind = what[:3]
                    y = {"lny": ya, "lnf": yf}[kind]
                    wait(act, nmr_done[kind], b, 2, n + 1)
                    for kb in range(HB * n, HB * (n + 1)):
                        last = nc.scalar.activation(y[:, kb, :], y[:, kb, :], ACT.Identity,
                                                    bias=nmr[kind][:, kb:kb + 1],
                                                    scale=rstd[kind][:, kb:kb + 1])
                    last.then_inc(norm_done[kind], 1)

            def step(i):
                for s in range(SLOTS):
                    for t in range(TURNS):
                        exponentials(i, s, t)
                        if s % 2 == 0 and t == READ_TURN:
                            read_output(i, s)
                        for what, n, off in SCHEDULE.get((s, t), []):
                            if there(i + off):
                                job(what, n, i + off)

            steps(act, step, setup)
            for n in range(2):
                act.wait_ge(stored[n], 16 * NB)

        @block.vector
        def _(dve):
            def first_weights():
                dve.wait_ge(hi_split, 1)
                nc.vector.tensor_tensor(w_lo[:, 0:O_W1], w_stage[:, 0:O_W1], w_hi[:, 0:O_W1].bitcast(F32),
                                        ALU.subtract).then_inc(lo_split, 1)
                dve.wait_ge(rows_raw_in, 16)
                nc.vector.tensor_copy(rows_f32r.bitcast(F32R), rows_raw).then_inc(rows_set, 1)
                dve.wait_ge(c_in, 96)

            def setup(i):
                if i == 0:
                    for n, (lo, hi, src) in enumerate(W_REST):
                        dve.wait_ge(hi_split, 2 + n)
                        last = nc.vector.tensor_tensor(w_lo[:, lo:hi], src, w_hi[:, lo:hi].bitcast(F32),
                                                       ALU.subtract)
                        if n:
                            last.then_inc(lo_split, 1)
                    dve.wait_ge(consts, 2)

            def maxima(i, s, c):
                k, j = CH * s + c, s % 2
                wait(dve, max_mm, i, PC, k + 1)
                if c == 0:
                    wait(dve, mm["mt"], i, PAIRS, s - 1)
                if c < 2:
                    dst, src = neg_max[:, j, 0, c:c + 1], p_max[k % 2][:, :]
                else:
                    dst = neg_max[:, j, c - 1, :]
                    src = p_max[k % 2][:, :].rearrange("p (a n) -> p a n", a=2)
                nc.vector.tensor_reduce(dst, src, axis=AX.X, op=ALU.max, negate=True).then_inc(red_done, 1)

            def stats(kind, src, n, b):
                for kb in range(HB * n, HB * (n + 1)):
                    last = nc.vector.bn_stats(bn[kind][:, kb, :], src[:, kb, :])
                last.then_inc(bn_done[kind], 1)

            def mean_variance(kind, n, b):
                for kb in range(HB * n, HB * (n + 1)):
                    last = nc.vector.bn_aggr(mv[kind][:, kb, :], bn[kind][:, kb, :])
                last.then_inc(mv_done[kind], 1)

            def minus_mean(kind, n, b):
                wait(dve, rstd_done[kind], b, 2, n + 1)
                at = slice(HB * n, HB * (n + 1))
                nc.vector.scalar_tensor_tensor(nmr[kind][:, at], mv[kind][:, at, 0], -1.0,
                                               rstd[kind][:, at], ALU.mult, ALU.mult)\
                    .then_inc(nmr_done[kind], 1)

            def normalise(kind, dst, src, n, b):
                wait(dve, rstd_done[kind], b, 2, n + 1)
                for kb in range(HB * n, HB * (n + 1)):
                    last = nc.vector.tensor_scalar(dst[:, kb, :], src[:, kb, :], mv[kind][:, kb, 0:1],
                                                   rstd[kind][:, kb:kb + 1], ALU.subtract, ALU.mult)
                last.then_inc(norm_done[kind], 1)

            def job(what, n, b):
                src = bank(what, n) if what in LINEAR else None
                if what == "mt":
                    wait(dve, mm["mt"], b, PAIRS, n + 1)
                    wait(dve, row_in, b, 128, 16 * n)
                    nc.vector.tensor_tensor(
                        max_row[:, :].bitcast(F32R).rearrange("r (k n) -> r k n", n=P),
                        src[0:2 * KB, 0:P].unsqueeze(1).broadcast_to([2 * KB, KB, P]),
                        own_block[:, :].rearrange("r (k n) -> r k n", n=P), ALU.mult).then_inc(ev["mt"], 1)
                elif what in ("x1t", "x2t", "o2t"):
                    if isinstance(b, int) and (what, n, b) == ("x1t", 0, 0):
                        first_weights()
                    parts = {"x1t": x1_t, "x2t": x2_t, "o2t": o2_t}[what]
                    wait(dve, hi_done[what], b, 2, n + 1)
                    nc.vector.tensor_tensor(parts[1][:, n, :], src[:, :], parts[0][:, n, :].bitcast(F32),
                                            ALU.subtract).then_inc(ev[what], 1)
                elif what == "qk":
                    wait(dve, hi_done["qk"], b, 4, n + 1)
                    nc.vector.scalar_tensor_tensor(qk[:, n // 2, 2 * (n % 2) + 1, :], src[:, :], bqk_s[:, n:n + 1],
                                                   qk[:, n // 2, 2 * (n % 2), :].bitcast(F32), ALU.add, ALU.subtract)\
                        .then_inc(ev["qk"], 1)
                elif what == "v":
                    wait(dve, mm["v"], b, 2, n + 1)
                    wait(dve, pv_mm, b, QC, 0)
                    for u in range(2):
                        last = nc.vector.tensor_tensor(
                            values[:, 2 * n + u, :, 0:HD],
                            src[:, u * D:(u + 1) * D].rearrange("p (h d) -> p h d", d=HD),
                            bv_s[:, :].rearrange("p (h d) -> p h d", d=HD), ALU.add)
                    last.then_inc(ev["v"], 1)
                elif what == "ot":
                    wait(dve, mm["ot"], b, 4, n + 1)
                    wait(dve, mm["o2t"], b, 2, 0)
                    sums = src[:, :].rearrange("p (k h c) -> p k h c", k=KB, c=VW)
                    nc.vector.reciprocal(den[:, :, :], sums[:, :, :, HD]).then_inc(den_done, 1)
                    wait(dve, den_done, b, 4, n + 1)
                    nc.vector.tensor_tensor(
                        o_n[:, :, n * 4 * HD:(n + 1) * 4 * HD].rearrange("p k (h d) -> p k h d", d=HD),
                        sums[:, :, :, 0:HD],
                        den[:, :, :].unsqueeze(3).broadcast_to([P, KB, 4, HD]), ALU.mult)\
                        .then_inc(ev["ot"], 1)
                elif what == "op":
                    wait(dve, mm["op"], b, 2, n + 1)
                    wait(dve, x1_done, b - 1, 2, n + 1)
                    for u in range(2):
                        last = nc.vector.tensor_tensor(ya[:, 2 * n + u, :], src[:, u * D:(u + 1) * D],
                                                       bo_s[:, :], ALU.add)
                    last.then_inc(ev["op"], 1)
                elif what == "f2":
                    wait(dve, mm["f2"], b, 4, n + 1)
                    wait(dve, stored[n // 2], b, 16, 0)
                    nc.vector.tensor_tensor(yf[:, n, :], src[:, 0:D], b2_s[:, :], ALU.add)\
                        .then_inc(ev["f2"], 1)
                elif what.endswith("_mean"):
                    mean_variance(what[:3], n, b)
                elif what == "ln1_stats":
                    wait(dve, xa_in, b, 16, 16)
                    stats("ln1", xa, n, b)
                elif what == "ln1_apply":
                    normalise("ln1", xa, xa, n, b)
                elif what == "lny_stats":
                    wait(dve, ev["op"], b, 2, n + 1)
                    stats("lny", ya, n, b)
                elif what == "lny_apply":
                    minus_mean("lny", n, b)
                elif what == "ln2_stats":
                    wait(dve, x1_done, b, 2, n + 1)
                    stats("ln2", xr, n, b)
                elif what == "ln2_apply":
                    wait(dve, mm["x2t"], b, 2, 0)
                    normalise("ln2", xh, xr, n, b)
                elif what == "lnf_stats":
                    wait(dve, ev["f2"], b, 4, 2 * n + 2)
                    stats("lnf", yf, n, b)
                elif what == "lnf_apply":
                    minus_mean("lnf", n, b)

            def step(i):
                for s in range(SLOTS):
                    for t in range(TURNS):
                        for what, n, off in SCHEDULE.get((s, t), []):
                            if what.endswith("_mean") and there(i + off):
                                wait(dve, bn_done[what[:3]], i + off, 2, n + 1)
                        if there(i):
                            maxima(i, s, t)
                        for what, n, off in SCHEDULE.get((s, t), []):
                            if there(i + off):
                                job(what, n, i + off)

            steps(dve, step, setup)

        @block.gpsimd
        def _(pool):
            nc.gpsimd.memset(minus_half[:, :], -0.5)
            nc.gpsimd.memset(eps[:, :], EPS).then_inc(consts, 1)
            nc.gpsimd.memset(values[:, :, :, :], 1.0).then_inc(consts, 1)
            pool.wait_ge(consts, 2)

            def one_over_std(kind, n, b):
                at = slice(HB * n, HB * (n + 1))
                wait(pool, mv_done[kind], b, 2, n + 1)
                nc.gpsimd.tensor_tensor(ve[kind][:, at], mv[kind][:, at, 1], eps[:, at], ALU.add)\
                    .then_inc(ve_done[kind], 1)
                wait(pool, ve_done[kind], b, 2, n + 1)
                nc.gpsimd.tensor_tensor(rstd[kind][:, at], ve[kind][:, at], minus_half[:, at],
                                        ALU.pow).then_inc(rstd_done[kind], 1)

            def job(what, n, b):
                if what.endswith("_mean"):
                    one_over_std(what[:3], n, b)
                elif what == "f1":
                    wait(pool, ev["f1"], b, 8, n + 1)
                    for u in range(2):
                        m = 2 * (n % 4) + u
                        last = nc.gpsimd.tensor_tensor(h_parts[1][:, m, :], h_f[:, n % 2, u, :],
                                                       h_parts[0][:, m, :].bitcast(F32), ALU.subtract)
                    last.then_inc(h_lo, 1)
                elif what == "lny_apply":
                    wait(pool, xr_in, b, 16, 16)
                    wait(pool, norm_done["lny"], b, 2, n + 1)
                    at = slice(HB * n, HB * (n + 1))
                    nc.gpsimd.tensor_tensor(xr[:, at, :], xr[:, at, :], ya[:, at, :], ALU.add)\
                        .then_inc(x1_done, 1)
                elif what == "lnf_apply":
                    wait(pool, x1_kept, b, 2, n + 1)
                    wait(pool, norm_done["lnf"], b, 2, n + 1)
                    at = slice(2 * n, 2 * n + 2)
                    nc.gpsimd.tensor_tensor(yf[:, at, :], yf[:, at, :], x1_old[:, at, :], ALU.add)\
                        .then_inc(final, 1)

            def step(i):
                for s in range(SLOTS):
                    for t in range(TURNS):
                        for what, n, off in SCHEDULE.get((s, t), []):
                            if there(i + off):
                                job(what, n, i + off)

            steps(pool, step, lambda i: None)


def kernel(L0_attn_x, L0_attn_w_qkv, L0_attn_b_qkv, L0_attn_w_out, L0_attn_b_out,
           L0_ffn_W1, L0_ffn_b1, L0_ffn_W2, L0_ffn_b2):
    import numpy as np
    import concourse.bacc as bacc
    from concourse.bass_utils import run_bass_kernel_spmd

    P = 128
    x = np.ascontiguousarray(L0_attn_x)
    D = x.shape[2]
    b_qkv, b1 = np.asarray(L0_attn_b_qkv), np.asarray(L0_ffn_b1)

    def rows(a):
        return np.ascontiguousarray(np.broadcast_to(np.asarray(a), (P, D)))

    KB = x.shape[1] // P
    own_block = np.kron(np.eye(KB, dtype=np.float32), np.ones((2, P), np.float32))
    own_head = np.tile(np.kron(np.eye(2, dtype=np.float32), np.ones((1, KB * P), np.float32)), (KB, 1))

    b_qk = np.ascontiguousarray(b_qkv[:2 * D].reshape(2, D // P, P).transpose(2, 1, 0).reshape(P, 4))
    arrays = {
        "x": x,
        "w_qkv_t": np.ascontiguousarray(np.asarray(L0_attn_w_qkv).T),
        "b_qk": b_qk,
        "b_v": rows(b_qkv[2 * D:]),
        "w_out_t": np.ascontiguousarray(np.asarray(L0_attn_w_out).T),
        "b_out": rows(L0_attn_b_out),
        "w1": np.ascontiguousarray(L0_ffn_W1),
        "b1": np.ascontiguousarray(b1.reshape(-1, P).T),
        "w2": np.ascontiguousarray(L0_ffn_W2),
        "b2": rows(L0_ffn_b2),
        "ident_in": np.eye(P, dtype=np.float32),
        "own_block_in": own_block,
        "stack_rows_in": np.concatenate([np.zeros_like(own_head), own_head]),
    }
    nc = bacc.Bacc("TRN2", target_bir_lowering=False, num_devices=1)
    args = [nc.dram_tensor(name, a.shape, mybir.dt.from_np(a.dtype), kind="ExternalInput").ap()
            for name, a in arrays.items()]
    out = nc.dram_tensor("out", x.shape, mybir.dt.float32, kind="ExternalOutput").ap()
    sandwich(nc, *args, out)
    res = run_bass_kernel_spmd(nc, [arrays], core_ids=[0])
    return res.results[0]["out"]
```
